# Optimizing a Trainium2 kernel written in Bass

```python
import numpy as np
import jax
import jax.numpy as jnp

def _softmax(x, axis=-1):
    return jax.nn.softmax(x, axis=axis)

def _gelu(x):
    return jax.nn.gelu(x, approximate=True)

def _silu(x):
    return jax.nn.silu(x)

def _sigmoid(x):
    return jax.nn.sigmoid(x)

def _layernorm(x, axis=-1, eps=1e-05):
    m = jnp.mean(x, axis=axis, keepdims=True)
    v = jnp.var(x, axis=axis, keepdims=True)
    return (x - m) / jnp.sqrt(v + eps)

def _scatter_add(tgt, idx, src, axis=0):
    return tgt.at[idx].add(src)

def _segment_sum(src, seg, n):
    return jax.ops.segment_sum(src, seg, n)
kernel_name = 'mk_macaron_d1_jaxref_r8_10ed35'

def setup_inputs(seed: int=0):
    np.random.seed(seed)
    _w = jnp.asarray

    def _L0_attn_setup():
        import jax, jax.numpy as jnp
        import numpy as np
        D_MODEL = 128
        BATCH = 8
        SEQ = 256
        LN_EPS = 1e-05

        def _layernorm(z, w, b):
            m = jnp.mean(z, axis=-1, keepdims=True)
            v = jnp.mean(jnp.square(z - m), axis=-1, keepdims=True)
            return (z - m) * jax.lax.rsqrt(v + LN_EPS) * w + b

        def _reference_tuple_inner(x, ln_w, ln_b, tmk, tmv, tmr, decay_w, Wk, Wv, Wr, Wo):
            xn = _layernorm(x, ln_w, ln_b)
            prev = jnp.pad(xn[:, :-1, :], ((0, 0), (1, 0), (0, 0)))
            xk = xn * tmk + prev * (1.0 - tmk)
            xv = xn * tmv + prev * (1.0 - tmv)
            xr = xn * tmr + prev * (1.0 - tmr)
            k = jnp.einsum('btd,ed->bte', xk, Wk)
            v = jnp.einsum('btd,ed->bte', xv, Wv)
            r = jax.nn.sigmoid(jnp.einsum('btd,ed->bte', xr, Wr))
            decay = jax.nn.sigmoid(decay_w)
            kv = (k * v).swapaxes(0, 1)

            def step(S, kv_t):
                S_new = decay * S + kv_t
                return (S_new, S_new)
            S0 = jnp.zeros((x.shape[0], x.shape[2]), x.dtype)
            final_S, S_seq = jax.lax.scan(step, S0, kv)
            S_seq = S_seq.swapaxes(0, 1)
            out = x + r * jnp.einsum('btd,ed->bte', S_seq, Wo)
            return (out, final_S, S_seq)
        key = jax.random.key(seed)
        ks = jax.random.split(key, 8)
        scale = 0.1 / np.sqrt(D_MODEL)
        x = jax.random.normal(ks[0], (BATCH, SEQ, D_MODEL), dtype=jnp.float32)
        return {'x': x, 'ln_w': jnp.ones((D_MODEL,), jnp.float32), 'ln_b': jnp.zeros((D_MODEL,), jnp.float32), 'tmk': jnp.ones((D_MODEL,), jnp.float32) * 0.9, 'tmv': jnp.ones((D_MODEL,), jnp.float32) * 0.9, 'tmr': jnp.ones((D_MODEL,), jnp.float32) * 0.9, 'decay_w': jnp.full((D_MODEL,), -0.5, jnp.float32) + 0.1 * jax.random.normal(ks[1], (D_MODEL,), jnp.float32), 'Wk': scale * jax.random.normal(ks[2], (D_MODEL, D_MODEL), jnp.float32), 'Wv': scale * jax.random.normal(ks[3], (D_MODEL, D_MODEL), jnp.float32), 'Wr': scale * jax.random.normal(ks[4], (D_MODEL, D_MODEL), jnp.float32), 'Wo': scale * jax.random.normal(ks[5], (D_MODEL, D_MODEL), jnp.float32)}
    _L0_attn_in = _L0_attn_setup()

    def _L0_ffn_setup():
        import jax, jax.numpy as jnp
        import numpy as np
        from jax import lax
        T, B, I, M, O = (32, 64, 128, 128, 128)

        def _xavier(key, shape):
            fan_out, fan_in = shape
            limit = float(np.sqrt(6.0 / (fan_in + fan_out)))
            return jax.random.uniform(key, shape, jnp.float32, -limit, limit)
        key = jax.random.key(seed)
        ks = jax.random.split(key, 9)
        x = jax.random.normal(ks[0], (T, B, I), jnp.float32)
        return {'x': x, 'wf': _xavier(ks[1], (M, I)), 'uf': _xavier(ks[2], (M, M)), 'bf': jnp.zeros((M,), jnp.float32), 'wi': _xavier(ks[3], (M, I)), 'ui': _xavier(ks[4], (M, M)), 'bi': jnp.zeros((M,), jnp.float32), 'wc': _xavier(ks[5], (M, I)), 'uc': _xavier(ks[6], (M, M)), 'bc': jnp.zeros((M,), jnp.float32), 'wo': _xavier(ks[7], (O, I)), 'uo': _xavier(ks[8], (O, M)), 'bo': jnp.zeros((O,), jnp.float32), 'in_c': jnp.zeros((M,), jnp.float32)}
    _L0_ffn_in = _L0_ffn_setup()
    _d = {'L0_attn_x': _L0_attn_in['x'], 'L0_attn_ln_w': _L0_attn_in['ln_w'], 'L0_attn_ln_b': _L0_attn_in['ln_b'], 'L0_attn_tmk': _L0_attn_in['tmk'], 'L0_attn_tmv': _L0_attn_in['tmv'], 'L0_attn_tmr': _L0_attn_in['tmr'], 'L0_attn_decay_w': _L0_attn_in['decay_w'], 'L0_attn_Wk': _L0_attn_in['Wk'], 'L0_attn_Wv': _L0_attn_in['Wv'], 'L0_attn_Wr': _L0_attn_in['Wr'], 'L0_attn_Wo': _L0_attn_in['Wo'], 'L0_ffn_wf': _L0_ffn_in['wf'], 'L0_ffn_uf': _L0_ffn_in['uf'], 'L0_ffn_bf': _L0_ffn_in['bf'], 'L0_ffn_wi': _L0_ffn_in['wi'], 'L0_ffn_ui': _L0_ffn_in['ui'], 'L0_ffn_bi': _L0_ffn_in['bi'], 'L0_ffn_wc': _L0_ffn_in['wc'], 'L0_ffn_uc': _L0_ffn_in['uc'], 'L0_ffn_bc': _L0_ffn_in['bc'], 'L0_ffn_wo': _L0_ffn_in['wo'], 'L0_ffn_uo': _L0_ffn_in['uo'], 'L0_ffn_bo': _L0_ffn_in['bo'], 'L0_ffn_in_c': _L0_ffn_in['in_c']}
    _x0 = _d['L0_attn_x']
    _d['L0_attn_x'] = jax.random.normal(jax.random.fold_in(jax.random.key(seed), 1), (8, 512, 128), dtype=_x0.dtype)
    del _x0
    return _d

def reference(L0_attn_x, L0_attn_ln_w, L0_attn_ln_b, L0_attn_tmk, L0_attn_tmv, L0_attn_tmr, L0_attn_decay_w, L0_attn_Wk, L0_attn_Wv, L0_attn_Wr, L0_attn_Wo, L0_ffn_wf, L0_ffn_uf, L0_ffn_bf, L0_ffn_wi, L0_ffn_ui, L0_ffn_bi, L0_ffn_wc, L0_ffn_uc, L0_ffn_bc, L0_ffn_wo, L0_ffn_uo, L0_ffn_bo, L0_ffn_in_c):

    def _L0_attn_ref(x, ln_w, ln_b, tmk, tmv, tmr, decay_w, Wk, Wv, Wr, Wo):
        import jax, jax.numpy as jnp
        import numpy as np
        D_MODEL = 128
        BATCH = 8
        SEQ = 256
        LN_EPS = 1e-05

        def _layernorm(z, w, b):
            m = jnp.mean(z, axis=-1, keepdims=True)
            v = jnp.mean(jnp.square(z - m), axis=-1, keepdims=True)
            return (z - m) * jax.lax.rsqrt(v + LN_EPS) * w + b

        def _reference_tuple_inner(x, ln_w, ln_b, tmk, tmv, tmr, decay_w, Wk, Wv, Wr, Wo):
            xn = _layernorm(x, ln_w, ln_b)
            prev = jnp.pad(xn[:, :-1, :], ((0, 0), (1, 0), (0, 0)))
            xk = xn * tmk + prev * (1.0 - tmk)
            xv = xn * tmv + prev * (1.0 - tmv)
            xr = xn * tmr + prev * (1.0 - tmr)
            k = jnp.einsum('btd,ed->bte', xk, Wk)
            v = jnp.einsum('btd,ed->bte', xv, Wv)
            r = jax.nn.sigmoid(jnp.einsum('btd,ed->bte', xr, Wr))
            decay = jax.nn.sigmoid(decay_w)
            kv = (k * v).swapaxes(0, 1)

            def step(S, kv_t):
                S_new = decay * S + kv_t
                return (S_new, S_new)
            S0 = jnp.zeros((x.shape[0], x.shape[2]), x.dtype)
            final_S, S_seq = jax.lax.scan(step, S0, kv)
            S_seq = S_seq.swapaxes(0, 1)
            out = x + r * jnp.einsum('btd,ed->bte', S_seq, Wo)
            return (out, final_S, S_seq)
        return _reference_tuple_inner(x, ln_w, ln_b, tmk, tmv, tmr, decay_w, Wk, Wv, Wr, Wo)[0]

    def _L0_ffn_ref(x, wf, uf, bf, wi, ui, bi, wc, uc, bc, wo, uo, bo, in_c):
        import jax, jax.numpy as jnp
        import numpy as np
        from jax import lax
        T, B, I, M, O = (32, 64, 128, 128, 128)

        def _xavier(key, shape):
            fan_out, fan_in = shape
            limit = float(np.sqrt(6.0 / (fan_in + fan_out)))
            return jax.random.uniform(key, shape, jnp.float32, -limit, limit)
        batch = x.shape[1]
        c0 = jnp.broadcast_to(in_c, (batch, in_c.shape[0]))

        def step(c, xt):
            ft = jax.nn.sigmoid(xt @ wf.T + c @ uf.T + bf)
            it = jax.nn.sigmoid(xt @ wi.T + c @ ui.T + bi)
            gt = jnp.tanh(xt @ wc.T + c @ uc.T + bc)
            c = ft * c + it * gt
            return (c, None)
        c_final, _ = lax.scan(step, c0, x)
        h = jnp.tanh(jnp.einsum('tbi,oi->tbo', x, wo) + c_final @ uo.T + bo)
        return h
    x = L0_attn_x
    x = x + 0.5 * _L0_ffn_ref(_layernorm(x, axis=-1), L0_ffn_wf, L0_ffn_uf, L0_ffn_bf, L0_ffn_wi, L0_ffn_ui, L0_ffn_bi, L0_ffn_wc, L0_ffn_uc, L0_ffn_bc, L0_ffn_wo, L0_ffn_uo, L0_ffn_bo, L0_ffn_in_c)
    x = x + _L0_attn_ref(_layernorm(x, axis=-1), L0_attn_ln_w, L0_attn_ln_b, L0_attn_tmk, L0_attn_tmv, L0_attn_tmr, L0_attn_decay_w, L0_attn_Wk, L0_attn_Wv, L0_attn_Wr, L0_attn_Wo)
    x = x + 0.5 * _L0_ffn_ref(_layernorm(x, axis=-1), L0_ffn_wf, L0_ffn_uf, L0_ffn_bf, L0_ffn_wi, L0_ffn_ui, L0_ffn_bi, L0_ffn_wc, L0_ffn_uc, L0_ffn_bc, L0_ffn_wo, L0_ffn_uo, L0_ffn_bo, L0_ffn_in_c)
    return x

_drawn_inputs = setup_inputs


def setup_inputs(seed=0):
    import zlib

    import numpy as np

    out = dict(_drawn_inputs(seed))
    spreads = {'L0_attn_ln_w': (1.0, 0.6),
     'L0_attn_ln_b': (0.0, 0.8),
     'L0_attn_tmk': (0.8999999761581421, 0.6),
     'L0_attn_tmv': (0.8999999761581421, 0.6),
     'L0_attn_tmr': (0.8999999761581421, 0.6),
     'L0_ffn_bf': (0.0, 0.8),
     'L0_ffn_bi': (0.0, 0.8),
     'L0_ffn_bc': (0.0, 0.1),
     'L0_ffn_bo': (0.0, 0.1),
     'L0_ffn_in_c': (0.0, 0.8)}
    factors = {'L0_attn_decay_w': 200.0,
     'L0_attn_Wk': 8.0,
     'L0_attn_Wv': 8.0,
     'L0_attn_Wr': 8.0,
     'L0_attn_Wo': 8.0}
    for name, (base, spread) in spreads.items():
        noise = np.random.default_rng([zlib.crc32(name.encode()), seed]).standard_normal(out[name].shape)
        drawn = base * np.exp(spread * noise) if base else spread * noise
        out[name] = jnp.asarray(drawn.astype(out[name].dtype))
    for name, factor in factors.items():
        out[name] = (out[name] * factor).astype(out[name].dtype)
    return out
```

```python
from contextlib import ExitStack

import concourse.bass as bass
from concourse import mybir

F32 = mybir.dt.float32
F32R = mybir.dt.float32r
ALU = mybir.AluOpType
ACT = mybir.ActivationFunctionType

P = 128
T = 8
N = 512
NT = N // P
HALF = N // 2
EPS = 1e-5

WEIGHTS = ["wi", "wc", "wf", "wo", "ui", "uc", "uf", "uo", "Wk", "Wv", "Wr", "Wo"]
VECTORS = ["bi", "bc", "bf", "in_c", "decay_w", "ln_w", "ln_b", "tmk", "tmv", "tmr"]
GATES = 3


def macaron_kernel(nc, x, out, weights, vectors, bo):
    ctx = ExitStack()
    with ctx:
        def sb(name, shape, dt=F32):
            return ctx.enter_context(nc.sbuf_tensor(name, shape, dt))

        def sem(name):
            return ctx.enter_context(nc.semaphore(name))

        X = sb("X", [P, T, NT, P])
        XO = sb("XO", [P, T, NT, P])
        w_raw = sb("w_raw", [P, len(WEIGHTS), P])
        wx_hi, wx_lo = sb("wx_hi", [P, 4, P], F32R), sb("wx_lo", [P, 4, P], F32R)
        wc_hi, wc_lo = sb("wc_hi", [P, 4, P], F32R), sb("wc_lo", [P, 4, P], F32R)
        mix = sb("mix", [P, 6, P])
        mix_hi, mix_lo = sb("mix_hi", [P, 6, P], F32R), sb("mix_lo", [P, 6, P], F32R)
        wo_attn = sb("wo_attn", [P, P])
        v_rows, v_cols = sb("v_rows", [len(VECTORS), P]), sb("v_cols", [P, len(VECTORS)])
        bo_row, ones_row = sb("bo_row", [1, P]), sb("ones_row", [1, P])
        tm_cols = sb("tm_cols", [P, 6])
        decay = sb("decay", [P, 1])
        ident = sb("ident", [P, P])
        minus_half = sb("minus_half", [P, NT])
        bn = sb("bn", [P, 3, 2, NT, 6])
        mv = sb("mv", [P, 3, 2, NT, 2])
        sc = sb("sc", [P, 3, 2, 12, NT])
        y_rows = sb("y_rows", [P, 2, NT, P])
        x_hi, x_lo = sb("x_hi", [P, 2, N], F32R), sb("x_lo", [P, 2, N], F32R)
        gate = sb("gate", [P, GATES, N])
        ig, fc, c = sb("ig", [P, N]), sb("fc", [P, N]), sb("c", [P, N])
        c_hi, c_lo = sb("c_hi", [P, N], F32R), sb("c_lo", [P, N], F32R)
        cuo = sb("cuo", [P, NT, P])
        h = sb("h", [P, 2, NT, P])
        x1 = sb("x1", [P, 2, NT, P])
        z_rows = sb("z_rows", [P, 2, NT, P])
        res = sb("res", [P, 2, NT, P])
        a = sb("a", [P, N])
        a_hi, a_lo = sb("a_hi", [P, 2, N + 2], F32R), sb("a_lo", [P, 2, N + 2], F32R)
        k_sb, kv, s_sb = sb("k_sb", [P, N]), sb("kv", [P, N]), sb("s_sb", [P, N])
        r_sb, ro = sb("r_sb", [P, N]), sb("ro", [P, N])

        bank = [ctx.enter_context(nc.psum_tensor(f"bank{i}", [P, N], F32)) for i in range(8)]
        ps_t = bank[0]
        ps_xo = bank[1]
        ps_half = [bank[2:5], bank[5:8]]
        ps_k, ps_v, ps_r, ps_o = bank[1], bank[2], bank[3], bank[4]
        ps_gate = bank[5:8]

        S = {}

        def s(name):
            if name not in S:
                S[name] = sem(name)
            return S[name]

        V = {n: v_cols[:, i:i + 1] for i, n in enumerate(VECTORS)}
        gate_bias = [V["bi"], V["bc"], V["bf"]]
        gate_fn = [ACT.Sigmoid, ACT.Tanh, ACT.Sigmoid]

        def wait(eng, name, value):
            if isinstance(value, int) and value <= 0:
                return
            eng.wait_ge(s(name), value)

        def run_slots(eng, slot, first, loop_from, loop_to, last):
            for i in range(first, loop_from):
                slot(i, i % 2)
            if loop_to > loop_from:
                assert (loop_to - loop_from) % 2 == 0 and loop_from % 2 == 0
                if LOOPS:
                    with eng.Fori(loop_from, loop_to - 1, 2) as i:
                        slot(i, 0)
                        slot(i + 1, 1)
                else:
                    for i in range(loop_from, loop_to):
                        slot(i, i % 2)
            for i in range(loop_to, last):
                slot(i, i % 2)

        def flat(tile):
            return tile.rearrange("p n d -> p (n d)")

        block = ctx.enter_context(nc.Block())

        def load_weight(eng, name):
            i = WEIGHTS.index(name)
            eng.dma_start(w_raw[:, i, :], weights[name]).then_inc(s(f"w_loaded{i // 4}"), 16)

        @block.sync
        def _(sp):
            xr = x.rearrange("t (n p) d -> t p n d", p=P)
            orr = out.rearrange("t (n p) d -> t p n d", p=P)
            sp.dma_start(X[:, 0], xr[0]).then_inc(s("x0_loaded"), 16)
            for name in WEIGHTS[0:4]:
                load_weight(sp, name)
            sp.dma_start(X[:, 1], xr[1]).then_inc(s("x1_loaded"), 16)
            for t in range(2, T):
                sp.dma_start(X[:, t], xr[t]).then_inc(s("x_loaded"), 16)
            for name in WEIGHTS[8:12]:
                load_weight(sp, name)

            def store(t, _):
                wait(sp, "out_ready", t + 1)
                sp.dma_start(orr[t], X[:, t]).then_inc(s("stored"), 16)

            for t in range(T):
                store(t, 0)
            sp.wait_ge(s("stored"), 16 * T)

        @block.scalar
        def _(act):
            sc_e = nc.scalar
            for i, name in enumerate(VECTORS):
                act.dma_start(v_rows[i:i + 1, :], vectors[name].rearrange("(a n) -> a n", a=1)).then_inc(s("v_loaded"), 16)
            act.dma_start(bo_row[:], bo.rearrange("(a n) -> a n", a=1)).then_inc(s("v_loaded"), 16)
            for name in WEIGHTS[4:8]:
                load_weight(act, name)

            def normalise(dst, src, ln, par, scale_at, bias_at, done):
                for n in range(NT):
                    i = sc_e.activation(dst[:, n], src[:, n], ACT.Identity,
                                        scale=sc[:, ln, par, scale_at, n:n + 1], bias=sc[:, ln, par, bias_at, n:n + 1])
                i.then_inc(s(done), 1)

            act.wait_ge(s("wx_t"), 1)
            sc_e.activation(flat(wx_hi[:]), bank[1][:], ACT.Copy).then_inc(s("wx_hi"), 1)
            act.wait_ge(s("wc_t"), 1)
            sc_e.activation(flat(wc_hi[:]), bank[2][:], ACT.Copy).then_inc(s("wc_hi"), 1)

            def y0(t, par):
                if isinstance(t, int) and t >= T:
                    return
                wait(act, "sc0", t + 1)
                wait(act, "t0", t - 1)
                normalise(y_rows[:, par], X[:, t], 0, par, 1, 3, "y0")

            def hi0(t, par):
                if isinstance(t, int) and t >= T:
                    return
                wait(act, "t0", t + 1)
                wait(act, "xo1_mm", t - 1)
                sc_e.activation(x_hi[:, par], ps_t[:], ACT.Copy).then_inc(s("x0_hi"), 1)

            y0(0, 0)
            hi0(0, 0)
            y0(1, 1)

            def slot0(t, par):
                for hf in range(2):
                    cols = slice(hf * HALF, (hf + 1) * HALF)
                    for g in range(GATES):
                        wait(act, f"gate1_mm{hf}", GATES * t + g + 1)
                        wait(act, f"ig1_{hf}" if g < 2 else f"fc1_{hf}", t)
                        sc_e.activation(gate[:, g, cols], ps_half[hf][g][:, :HALF], gate_fn[g],
                                        bias=gate_bias[g]).then_inc(s(f"gate1_{hf}"), 1)
                    if hf == 0:
                        hi0(t + 1, 1 - par)
                y0(t + 2, par)
                wait(act, "xo1_mm", t + 1)
                sc_e.activation(flat(XO[:, t]), ps_xo[:], ACT.Copy).then_inc(s("xo1"), 1)

            run_slots(act, slot0, 0, 2, T - 2, T)

            wait(act, "cuo1_mm", 1)
            sc_e.activation(flat(cuo[:]), bank[1][:], ACT.Copy).then_inc(s("cuo1"), 1)
            act.wait_ge(s("tm_ready"), 1)
            act.wait_ge(s("wa_t"), 1)
            for j in range(3):
                for prev in range(2):
                    i = sc_e.activation(mix[:, 2 * j + prev], bank[2][:, j * P:(j + 1) * P], ACT.Copy,
                                        scale=tm_cols[:, 2 * j + prev:2 * j + prev + 1])
            i.then_inc(s("mix_ready"), 1)
            sc_e.activation(wo_attn[:], bank[2][:, 3 * P:], ACT.Copy).then_inc(s("wo_ready"), 1)
            sc_e.activation(decay[:], V["decay_w"], ACT.Sigmoid).then_inc(s("decay_ready"), 1)

            def tanh1(t, par):
                wait(act, "hpre1", t + 1)
                sc_e.activation(flat(h[:, par]), flat(h[:, par]), ACT.Tanh).then_inc(s("h1"), 1)

            def z1(t, par):
                wait(act, "sc1", t + 1)
                wait(act, "t1", t - 1)
                normalise(z_rows[:, par], x1[:, par], 1, par, 7, 8, "z1")
                wait(act, "sc1b", t + 1)
                wait(act, "x2", t - 1)
                normalise(res[:, par], x1[:, par], 1, par, 9, 10, "res1")

            def a1(t, par):
                wait(act, "t1", t + 1)
                wait(act, "a_lo", t)
                sc_e.activation(a[:], ps_t[:], ACT.Identity, scale=V["ln_w"], bias=V["ln_b"]).then_inc(s("a"), 1)

            tanh1(0, 0)
            z1(0, 0)
            a1(0, 0)

            def slot1(t, par):
                tp, qpar = t - 1, 1 - par
                now = not (isinstance(t, int) and t >= T)
                nxt = not (isinstance(t, int) and t + 1 >= T)
                before = not (isinstance(t, int) and t < 1)
                if nxt:
                    tanh1(t + 1, qpar)
                if before:
                    wait(act, "sc2", tp + 1)
                    wait(act, "t2", tp - 1)
                    normalise(y_rows[:, qpar], X[:, tp], 2, qpar, 1, 3, "y2")
                if now:
                    wait(act, "k_mm", t + 1)
                    wait(act, "kv", t)
                    sc_e.activation(k_sb[:], ps_k[:], ACT.Copy).then_inc(s("k"), 1)
                    wait(act, "r_mm", t + 1)
                    wait(act, "ro", t)
                    sc_e.activation(r_sb[:], ps_r[:], ACT.Sigmoid).then_inc(s("r"), 1)
                if before:
                    wait(act, "t2", tp + 1)
                    wait(act, "xo2_mm", tp - 1)
                    sc_e.activation(x_hi[:, qpar], ps_t[:], ACT.Copy).then_inc(s("x2_hi"), 1)
                if nxt:
                    z1(t + 1, qpar)
                    a1(t + 1, qpar)
                if before:
                    for g in range(GATES):
                        wait(act, "gate2_mm", GATES * tp + g + 1)
                        wait(act, "ig2" if g < 2 else "fc2", tp)
                        sc_e.activation(gate[:, g], ps_gate[g][:], gate_fn[g],
                                        bias=gate_bias[g]).then_inc(s("gate2"), 1)
                    wait(act, "xo2_mm", tp + 1)
                    sc_e.activation(flat(XO[:, tp]), ps_r[:], ACT.Copy).then_inc(s("xo2"), 1)

            run_slots(act, slot1, 0, 2, 6, T + 1)

            wait(act, "cuo2_mm", 1)
            sc_e.activation(flat(cuo[:]), bank[1][:], ACT.Copy).then_inc(s("cuo2"), 1)

            def slot2(t, par):
                wait(act, "hpre2_even" if par == 0 else "hpre2_odd", (t - par) // 2 + 1 if isinstance(t, int) else t)
                sc_e.activation(flat(h[:, par]), flat(h[:, par]), ACT.Tanh).then_inc(s("h2"), 1)

            for t in range(T):
                slot2(t, t % 2)

        @block.gpsimd
        def _(pool):
            g_e = nc.gpsimd
            g_e.memset(ident[:], 0.0).then_inc(s("pool_init"), 1)
            g_e.memset(minus_half[:], -0.5).then_inc(s("pool_init"), 1)
            g_e.memset(ones_row[:], 1.0).then_inc(s("ones_ready"), 1)
            pool.wait_ge(s("pool_init"), 2)
            g_e.affine_select(out=ident[:], in_=ident[:], compare_op=ALU.not_equal, fill=1.0,
                              base=0, pattern=[[-1, P]], channel_multiplier=1).then_inc(s("ident_ready"), 1)

            def chain(ops, own, t, done_at):
                for n, op in enumerate(ops):
                    i = op()
                    if n + 1 in done_at:
                        i.then_inc(s(done_at[n + 1]), 1)
                        if n + 1 < len(ops):
                            wait(pool, done_at[n + 1], t + 1)
                    else:
                        i.then_inc(s(own), 1)
                        wait(pool, own, (len(ops) - len(done_at)) * t + n + 1 - sum(d <= n for d in done_at))

            def scalars(ln, t, par, own, done, used):
                mean, var = mv[:, ln, par, :, 0], mv[:, ln, par, :, 1]
                q = [sc[:, ln, par, i] for i in range(12)]
                wait(pool, used, t - 1)
                chain([
                    lambda: g_e.tensor_scalar(q[0], var, 1.0, EPS, ALU.mult, ALU.add),
                    lambda: g_e.tensor_tensor(q[1], q[0], minus_half[:], ALU.pow),
                    lambda: g_e.tensor_tensor(q[2], mean, q[1], ALU.mult),
                    lambda: g_e.tensor_scalar(q[3], q[2], -1.0, 0.0, ALU.mult, ALU.add),
                ], own, t, {4: done})

            def scalars1(t, par):
                mean, var = mv[:, 1, par, :, 0], mv[:, 1, par, :, 1]
                q = [sc[:, 1, par, i] for i in range(12)]
                wait(pool, "res1", t - 1)
                chain([
                    lambda: g_e.tensor_scalar(q[0], var, 1.0, EPS, ALU.mult, ALU.add),
                    lambda: g_e.tensor_tensor(q[1], q[0], minus_half[:], ALU.pow),
                    lambda: g_e.tensor_tensor(q[2], var, q[1], ALU.mult),
                    lambda: g_e.tensor_tensor(q[3], q[2], q[1], ALU.mult),
                    lambda: g_e.tensor_scalar(q[4], q[3], 1.0, EPS, ALU.mult, ALU.add),
                    lambda: g_e.tensor_tensor(q[5], q[4], minus_half[:], ALU.pow),
                    lambda: g_e.tensor_scalar(q[6], mean, -1.0, 0.0, ALU.mult, ALU.add),
                    lambda: g_e.tensor_tensor(q[7], q[1], q[5], ALU.mult),
                    lambda: g_e.tensor_tensor(q[8], q[6], q[7], ALU.mult),
                    lambda: g_e.tensor_scalar(q[9], q[1], 1.0, 1.0, ALU.mult, ALU.add),
                    lambda: g_e.tensor_tensor(q[10], q[6], q[1], ALU.mult),
                ], "own1", t, {9: "sc1", 11: "sc1b"})

            def sc0(t, par):
                if isinstance(t, int) and t >= T:
                    return
                wait(pool, "mv0", t + 1)
                scalars(0, t, par, "own0", "sc0", "y0")

            for t in range(2):
                sc0(t, t % 2)

            def slot0(t, par):
                for hf in range(2):
                    cols = slice(hf * HALF, (hf + 1) * HALF)
                    wait(pool, f"gate1_{hf}", GATES * t + 2)
                    wait(pool, f"c1_{hf}", t)
                    g_e.tensor_tensor(ig[:, cols], gate[:, 0, cols], gate[:, 1, cols],
                                      ALU.mult).then_inc(s(f"ig1_{hf}"), 1)
                    if hf == 0:
                        sc0(t + 2, par)

            run_slots(pool, slot0, 0, 2, T - 2, T)

            def hpre(t, par, done, h_read):
                wait(pool, h_read, t - 1)
                g_e.tensor_tensor(flat(h[:, par]), flat(XO[:, t]), flat(cuo[:]), ALU.add).then_inc(s(done), 1)

            wait(pool, "cuo1", 1)
            hpre(0, 0, "hpre1", "x1")
            wait(pool, "mv1", 1)
            scalars1(0, 0)
            hpre(1, 1, "hpre1", "x1")

            def slot1(t, par):
                tp, qpar = t - 1, 1 - par
                nxt = not (isinstance(t, int) and t + 1 >= T)
                nxt2 = not (isinstance(t, int) and t + 2 >= T)
                before = not (isinstance(t, int) and t < 1)
                if before:
                    wait(pool, "mv2", tp + 1)
                    scalars(2, tp, qpar, "own2", "sc2", "y2")
                if nxt:
                    wait(pool, "mv1", t + 2)
                    scalars1(t + 1, qpar)
                if nxt2:
                    hpre(t + 2, par, "hpre1", "x1")
                if before:
                    wait(pool, "gate2", GATES * tp + 2)
                    wait(pool, "c2", tp)
                    g_e.tensor_tensor(ig[:], gate[:, 0], gate[:, 1], ALU.mult).then_inc(s("ig2"), 1)

            run_slots(pool, slot1, 0, 2, 6, T + 1)

            wait(pool, "cuo2", 1)
            for t in range(0, T, 2):
                hpre(t, 0, "hpre2_even", "out_ready")

        @block.vector
        def _(dve):
            v_e = nc.vector

            def stats(src, ln, t, par, own, done, used):
                wait(dve, used, t - 1)
                for n in range(NT):
                    i = v_e.bn_stats(bn[:, ln, par, n], src[:, n])
                i.then_inc(s(own), 1)
                wait(dve, own, t + 1)
                for n in range(NT):
                    i = v_e.bn_aggr(mv[:, ln, par, n], bn[:, ln, par, n])
                i.then_inc(s(done), 1)

            def stats0(t, par):
                if isinstance(t, int) and t >= T:
                    return
                stats(X[:, t], 0, t, par, "bn0", "mv0", "sc0")

            def lo0(t, par):
                if isinstance(t, int) and t >= T:
                    return
                wait(dve, "x0_hi", t + 1)
                v_e.tensor_tensor(x_lo[:, par], ps_t[:], x_hi[:, par].bitcast(F32),
                                  ALU.subtract).then_inc(s("x0_lo"), 1)

            v_e.memset(a_hi[:, :, 0:2].bitcast(F32), 0.0)
            v_e.memset(a_lo[:, :, 0:2].bitcast(F32), 0.0).then_inc(s("pad_ready"), 1)
            dve.wait_ge(s("x0_loaded"), 16)
            stats0(0, 0)
            dve.wait_ge(s("v_t"), 1)
            v_e.tensor_copy(v_cols[:], bank[3][:, 0:len(VECTORS)]).then_inc(s("v_ready"), 1)
            dve.wait_ge(s("v_ready"), 1)
            v_e.tensor_copy(c[:], V["in_c"].to_broadcast([P, N])).then_inc(s("c_init"), 1)
            dve.wait_ge(s("c_init"), 1)
            v_e.tensor_copy(c_hi[:], c[:]).then_inc(s("c_init"), 1)
            dve.wait_ge(s("c_init"), 2)
            v_e.tensor_tensor(c_lo[:], c[:], c_hi[:].bitcast(F32), ALU.subtract).then_inc(s("c_init"), 1)
            dve.wait_ge(s("wx_hi"), 1)
            v_e.tensor_tensor(flat(wx_lo[:]), bank[1][:], flat(wx_hi[:]).bitcast(F32), ALU.subtract).then_inc(s("wx_ready"), 1)
            dve.wait_ge(s("wc_hi"), 1)
            v_e.tensor_tensor(flat(wc_lo[:]), bank[2][:], flat(wc_hi[:]).bitcast(F32), ALU.subtract).then_inc(s("wc_ready"), 1)
            lo0(0, 0)
            dve.wait_ge(s("x1_loaded"), 16)
            stats0(1, 1)
            dve.wait_ge(s("x_loaded"), 16 * (T - 2))
            stats0(2, 0)

            def slot0(t, par):
                for hf in range(2):
                    cols = slice(hf * HALF, (hf + 1) * HALF)
                    wait(dve, f"gate1_{hf}", GATES * (t + 1))
                    v_e.tensor_tensor(fc[:, cols], gate[:, 2, cols], c[:, cols], ALU.mult).then_inc(s(f"fc1_{hf}"), 1)
                    wait(dve, f"fc1_{hf}", t + 1)
                    wait(dve, f"ig1_{hf}", t + 1)
                    v_e.tensor_tensor(c[:, cols], fc[:, cols], ig[:, cols], ALU.add).then_inc(s(f"c1_{hf}"), 1)
                    wait(dve, f"c1_{hf}", t + 1)
                    v_e.tensor_copy(c_hi[:, cols], c[:, cols]).then_inc(s(f"c1_hi{hf}"), 1)
                    wait(dve, f"c1_hi{hf}", t + 1)
                    v_e.tensor_tensor(c_lo[:, cols], c[:, cols], c_hi[:, cols].bitcast(F32),
                                      ALU.subtract).then_inc(s(f"c1_lo{hf}"), 1)
                    if hf == 0:
                        lo0(t + 1, 1 - par)
                stats0(t + 3, 1 - par)

            run_slots(dve, slot0, 0, 2, T - 4, T)

            for j, name in enumerate(("tmk", "tmv", "tmr")):
                v_e.tensor_copy(tm_cols[:, 2 * j:2 * j + 1], V[name])
                i = v_e.tensor_scalar(tm_cols[:, 2 * j + 1:2 * j + 2], V[name], -1.0, 1.0, ALU.mult, ALU.add)
            i.then_inc(s("tm_ready"), 1)
            dve.wait_ge(s("mix_ready"), 1)
            v_e.tensor_copy(flat(mix_hi[:]), flat(mix[:])).then_inc(s("mix_hi"), 1)
            dve.wait_ge(s("mix_hi"), 1)
            v_e.tensor_tensor(flat(mix_lo[:]), flat(mix[:]), flat(mix_hi[:]).bitcast(F32), ALU.subtract).then_inc(s("mix_lo"), 1)
            dve.wait_ge(s("decay_ready"), 1)

            def front1(t, par):
                wait(dve, "h1", t + 1)
                wait(dve, "res1", t - 1)
                v_e.scalar_tensor_tensor(out=flat(x1[:, par]), in0=flat(h[:, par]), scalar=0.5, in1=flat(X[:, t]),
                                         op0=ALU.mult, op1=ALU.add).then_inc(s("x1"), 1)
                wait(dve, "x1", t + 1)
                stats(x1[:, par], 1, t, par, "bn1", "mv1", "sc1b")

            def split_a(t, par):
                wait(dve, "a", t + 1)
                wait(dve, "r_mm", t - 1)
                v_e.tensor_copy(a_hi[:, par, 2:], a[:]).then_inc(s("a_hi"), 1)
                wait(dve, "a_hi", t + 1)
                v_e.tensor_tensor(a_lo[:, par, 2:], a[:], a_hi[:, par, 2:].bitcast(F32), ALU.subtract).then_inc(s("a_lo"), 1)

            front1(0, 0)
            split_a(0, 0)

            def slot1(t, par):
                tp, qpar = t - 1, 1 - par
                now = not (isinstance(t, int) and t >= T)
                nxt = not (isinstance(t, int) and t + 1 >= T)
                before = not (isinstance(t, int) and t < 1)
                if nxt:
                    front1(t + 1, qpar)
                if now:
                    wait(dve, "k", t + 1)
                    wait(dve, "v_mm", t + 1)
                    v_e.tensor_tensor(kv[:], ps_v[:], k_sb[:], ALU.mult).then_inc(s("kv"), 1)
                    wait(dve, "kv", t + 1)
                    wait(dve, "o_mm", t)
                    v_e.tensor_tensor_scan(s_sb[:], decay[:, 0:1].to_broadcast([P, N]), kv[:], 0.0,
                                           ALU.mult, ALU.add).then_inc(s("scan"), 1)
                    wait(dve, "o_mm", t + 1)
                    wait(dve, "r", t + 1)
                    wait(dve, "t3", t)
                    v_e.tensor_tensor(ro[:], ps_o[:], r_sb[:], ALU.mult).then_inc(s("ro"), 1)
                if before:
                    wait(dve, "x2_hi", tp + 1)
                    v_e.tensor_tensor(x_lo[:, qpar], ps_t[:], x_hi[:, qpar].bitcast(F32), ALU.subtract).then_inc(s("x2_lo"), 1)
                if now:
                    wait(dve, "t3", t + 1)
                    wait(dve, "res1", t + 1)
                    v_e.tensor_tensor(flat(X[:, t]), ps_o[:], flat(res[:, par]), ALU.add).then_inc(s("x2"), 1)
                if nxt:
                    split_a(t + 1, qpar)
                if now:
                    wait(dve, "x2", t + 1)
                    stats(X[:, t], 2, t, par, "bn2", "mv2", "sc2")
                if before:
                    wait(dve, "gate2", GATES * (tp + 1))
                    v_e.tensor_tensor(fc[:], gate[:, 2], c[:], ALU.mult).then_inc(s("fc2"), 1)
                    wait(dve, "fc2", tp + 1)
                    wait(dve, "ig2", tp + 1)
                    v_e.tensor_tensor(c[:], fc[:], ig[:], ALU.add).then_inc(s("c2"), 1)
                    wait(dve, "c2", tp + 1)
                    v_e.tensor_copy(c_hi[:], c[:]).then_inc(s("c2_hi"), 1)
                    wait(dve, "c2_hi", tp + 1)
                    v_e.tensor_tensor(c_lo[:], c[:], c_hi[:].bitcast(F32), ALU.subtract).then_inc(s("c2_lo"), 1)

            dve.wait_ge(s("cuo1_mm"), 1)
            v_e.tensor_copy(c[:], V["in_c"].to_broadcast([P, N])).then_inc(s("c_init"), 1)
            dve.wait_ge(s("c_init"), 4)
            v_e.tensor_copy(c_hi[:], c[:]).then_inc(s("c_init"), 1)
            dve.wait_ge(s("c_init"), 5)
            v_e.tensor_tensor(c_lo[:], c[:], c_hi[:].bitcast(F32), ALU.subtract).then_inc(s("c_init"), 1)

            run_slots(dve, slot1, 0, 2, 6, T + 1)

            dve.wait_ge(s("cuo2"), 1)

            def slot2(t, par):
                if par == 0:
                    wait(dve, "out_ready", t)
                    v_e.tensor_tensor(flat(h[:, 1]), flat(XO[:, t + 1]), flat(cuo[:]), ALU.add).then_inc(s("hpre2_odd"), 1)
                wait(dve, "h2", t + 1)
                v_e.scalar_tensor_tensor(out=flat(X[:, t]), in0=flat(h[:, par]), scalar=0.5, in1=flat(X[:, t]),
                                         op0=ALU.mult, op1=ALU.add).then_inc(s("out_ready"), 1)

            for t in range(T):
                slot2(t, t % 2)

        @block.tensor
        def _(pe):
            t_e = nc.tensor

            def product3(dst, w_hi, w_lo, r_hi, r_lo, start, stop):
                t_e.matmul(dst, w_hi, r_hi, start=start, stop=False)
                t_e.matmul(dst, w_lo, r_hi, start=False, stop=False)
                return t_e.matmul(dst, w_hi, r_lo, start=False, stop=stop)

            def transpose4(dst, src):
                for n in range(NT):
                    i = t_e.transpose(dst[:, n * P:(n + 1) * P], src[:, n], ident[:])
                return i

            def transpose_weights(first, dst, done):
                transpose4(dst, w_raw[:, first:first + 4]).then_inc(s(done), 1)

            pe.wait_ge(s("ident_ready"), 1)
            pe.wait_ge(s("w_loaded0"), 64)
            transpose_weights(0, bank[1], "wx_t")
            pe.wait_ge(s("v_loaded"), 16 * (len(VECTORS) + 1))
            nv = len(VECTORS)
            t_e.transpose(bank[3][:, 0:nv], v_rows[:], ident[0:nv, 0:nv]).then_inc(s("v_t"), 1)
            pe.wait_ge(s("w_loaded1"), 64)
            transpose_weights(4, bank[2], "wc_t")

            def t0(t, par):
                if isinstance(t, int) and t >= T:
                    return
                wait(pe, "y0", t + 1)
                wait(pe, "x0_lo", t)
                transpose4(ps_t, y_rows[:, par]).then_inc(s("t0"), 1)

            def project_rows(dst, par, done):
                for n in range(NT):
                    rows = slice(n * P, (n + 1) * P)
                    i = product3(dst[:, rows], x_hi[:, par, rows], x_lo[:, par, rows], wx_hi[:, 3], wx_lo[:, 3], True, True)
                i.then_inc(s(done), 1)

            def final_c(dst, done):
                for n in range(NT):
                    rows = slice(n * P, (n + 1) * P)
                    product3(dst[:, rows], c_hi[:, rows], c_lo[:, rows], wc_hi[:, 3], wc_lo[:, 3], True, False)
                    i = t_e.matmul(dst[:, rows], ones_row[:], bo_row[:], start=False, stop=True)
                i.then_inc(s(done), 1)

            t0(0, 0)
            pe.wait_ge(s("wx_ready"), 1)
            pe.wait_ge(s("wc_ready"), 1)
            pe.wait_ge(s("c_init"), 3)
            pe.wait_ge(s("ones_ready"), 1)

            def slot0(t, par):
                wait(pe, "x0_lo", t + 1)
                for hf in range(2):
                    cols = slice(hf * HALF, (hf + 1) * HALF)
                    wait(pe, f"c1_lo{hf}", t)
                    for g in range(GATES):
                        wait(pe, f"gate1_{hf}", GATES * (t - 1) + g + 1 if not isinstance(t, int) or t else 0)
                        dst = ps_half[hf][g][:, :HALF]
                        product3(dst, wx_hi[:, g], wx_lo[:, g], x_hi[:, par, cols], x_lo[:, par, cols], True, False)
                        product3(dst, wc_hi[:, g], wc_lo[:, g], c_hi[:, cols], c_lo[:, cols], False, True)\
                            .then_inc(s(f"gate1_mm{hf}"), 1)
                    if hf == 0:
                        t0(t + 1, 1 - par)
                wait(pe, "xo1", t)
                project_rows(ps_xo, par, "xo1_mm")

            run_slots(pe, slot0, 0, 2, T - 2, T)

            pe.wait_ge(s("c1_lo0"), T)
            pe.wait_ge(s("c1_lo1"), T)
            pe.wait_ge(s("xo1"), T)
            final_c(bank[1], "cuo1_mm")
            pe.wait_ge(s("w_loaded2"), 64)
            pe.wait_ge(s("gate1_0"), GATES * T)
            transpose_weights(8, bank[2], "wa_t")

            def t1(t, par):
                wait(pe, "z1", t + 1)
                wait(pe, "x2_lo", t - 1)
                transpose4(ps_t, z_rows[:, par]).then_inc(s("t1"), 1)

            def mixed(dst, j, par, done):
                row, prev = slice(2, N + 2), slice(1, N + 1)
                product3(dst, mix_hi[:, 2 * j], mix_lo[:, 2 * j], a_hi[:, par, row], a_lo[:, par, row], True, False)
                product3(dst, mix_hi[:, 2 * j + 1], mix_lo[:, 2 * j + 1], a_hi[:, par, prev], a_lo[:, par, prev],
                         False, True).then_inc(s(done), 1)

            t1(0, 0)
            pe.wait_ge(s("pad_ready"), 1)
            pe.wait_ge(s("mix_lo"), 1)
            pe.wait_ge(s("wo_ready"), 1)
            pe.wait_ge(s("cuo1"), 1)
            pe.wait_ge(s("c_init"), 6)

            def slot1(t, par):
                tp, qpar = t - 1, 1 - par
                now = not (isinstance(t, int) and t >= T)
                nxt = not (isinstance(t, int) and t + 1 >= T)
                before = not (isinstance(t, int) and t < 1)
                if now:
                    wait(pe, "a_lo", t + 1)
                    wait(pe, "k", t)
                    mixed(ps_k[:], 0, par, "k_mm")
                    wait(pe, "kv", t)
                    mixed(ps_v[:], 1, par, "v_mm")
                    wait(pe, "xo2", t - 1)
                    mixed(ps_r[:], 2, par, "r_mm")
                    wait(pe, "scan", t + 1)
                    wait(pe, "x2", t)
                    t_e.matmul(ps_o[:], wo_attn[:], s_sb[:], start=True, stop=True).then_inc(s("o_mm"), 1)
                if before:
                    wait(pe, "y2", tp + 1)
                    wait(pe, "a", t + 1 if not isinstance(t, int) else min(t + 1, T))
                    transpose4(ps_t, y_rows[:, qpar]).then_inc(s("t2"), 1)
                    wait(pe, "c2_lo", tp)
                    for g in range(GATES):
                        wait(pe, "gate2", GATES * (tp - 1) + g + 1 if not isinstance(t, int) or tp else 0)
                        product3(ps_gate[g][:], wc_hi[:, g], wc_lo[:, g], c_hi[:], c_lo[:], True, False)
                if now:
                    wait(pe, "ro", t + 1)
                    transpose4(ps_o, ro.rearrange("p (n d) -> p n d", n=NT)).then_inc(s("t3"), 1)
                if nxt:
                    t1(t + 1, qpar)
                if before:
                    wait(pe, "x2_lo", tp + 1)
                    for g in range(GATES):
                        product3(ps_gate[g][:], wx_hi[:, g], wx_lo[:, g], x_hi[:, qpar], x_lo[:, qpar], False, True)\
                            .then_inc(s("gate2_mm"), 1)
                    wait(pe, "r", t + 1 if not isinstance(t, int) else min(t + 1, T))
                    project_rows(ps_r, qpar, "xo2_mm")

            run_slots(pe, slot1, 0, 2, 6, T + 1)

            pe.wait_ge(s("c2_lo"), T)
            final_c(bank[1], "cuo2_mm")


LOOPS = False

_WEIGHTS = {"wi": "L0_ffn_wi", "wc": "L0_ffn_wc", "wf": "L0_ffn_wf", "wo": "L0_ffn_wo",
            "ui": "L0_ffn_ui", "uc": "L0_ffn_uc", "uf": "L0_ffn_uf", "uo": "L0_ffn_uo",
            "Wk": "L0_attn_Wk", "Wv": "L0_attn_Wv", "Wr": "L0_attn_Wr", "Wo": "L0_attn_Wo"}
_VECTORS = {"bi": "L0_ffn_bi", "bc": "L0_ffn_bc", "bf": "L0_ffn_bf", "in_c": "L0_ffn_in_c",
            "decay_w": "L0_attn_decay_w", "ln_w": "L0_attn_ln_w", "ln_b": "L0_attn_ln_b",
            "tmk": "L0_attn_tmk", "tmv": "L0_attn_tmv", "tmr": "L0_attn_tmr"}


def kernel(**inputs):
    import numpy as np
    import concourse.bacc as bacc
    from concourse.bass_utils import run_bass_kernel_spmd

    nc = bacc.Bacc("TRN2", target_bir_lowering=False, num_devices=1)
    arrays = {}

    def dram(name):
        arrays[name] = np.ascontiguousarray(inputs[name])
        return nc.dram_tensor(name, arrays[name].shape, mybir.dt.from_np(arrays[name].dtype), kind="ExternalInput").ap()

    x = dram("L0_attn_x")
    out = nc.dram_tensor("out", arrays["L0_attn_x"].shape, F32, kind="ExternalOutput").ap()
    macaron_kernel(nc, x, out, {k: dram(n) for k, n in _WEIGHTS.items()},
                   {k: dram(n) for k, n in _VECTORS.items()}, dram("L0_ffn_bo"))
    r = run_bass_kernel_spmd(nc, [arrays], core_ids=[0])
    return r.results[0]["out"]
```

```python
from contextlib import ExitStack

import concourse.bass as bass
from concourse import mybir

F32 = mybir.dt.float32
F32R = mybir.dt.float32r
ALU = mybir.AluOpType
ACT = mybir.ActivationFunctionType

P = 128
T = 8
N = 512
NT = N // P
HALF = N // 2
EPS = 1e-5

WARM = 3

WEIGHTS = ["wi", "wc", "wf", "wo", "ui", "uc", "uf", "uo", "Wk", "Wv", "Wr", "Wo"]
VECTORS = ["bi", "bc", "bf", "bo", "in_c", "decay_w", "ln_w", "ln_b", "tmk", "tmv", "tmr"]
GATES = 3


def macaron_kernel(nc, x, out, weights, vectors):
    ctx = ExitStack()
    with ctx:
        def sb(name, shape, dt=F32):
            return ctx.enter_context(nc.sbuf_tensor(name, shape, dt))

        def sem(name):
            return ctx.enter_context(nc.semaphore(name))

        X = sb("X", [P, T, NT, P])
        H = sb("H", [P, T, N])
        w_t = sb("w_t", [P, len(WEIGHTS), P])
        wx_hi, wx_lo = sb("wx_hi", [P, 4, P], F32R), sb("wx_lo", [P, 4, P], F32R)
        wc_hi, wc_lo = sb("wc_hi", [P, 4, P], F32R), sb("wc_lo", [P, 4, P], F32R)
        mix = sb("mix", [P, 6, P])
        mix_hi, mix_lo = sb("mix_hi", [P, 6, P], F32R), sb("mix_lo", [P, 6, P], F32R)
        v_cols = sb("v_cols", [P, len(VECTORS)])
        tm_cols = sb("tm_cols", [P, 6])
        decay = sb("decay", [P, 1])
        start_bias = sb("start_bias", [P, GATES])
        ident = sb("ident", [P, P])
        minus_half = sb("minus_half", [P, NT])
        bn = sb("bn", [P, 3, 2, NT, 6])
        mv = sb("mv", [P, 3, 2, NT, 2])
        sc = sb("sc", [P, 3, 2, 8, NT])
        zeros = sb("zeros", [P, NT, P])
        y_rows = sb("y_rows", [P, 2, NT, P])
        x_hi, x_lo = sb("x_hi", [P, T, N], F32R), sb("x_lo", [P, T, N], F32R)
        gate = sb("gate", [P, GATES, N])
        ig, fc, c = sb("ig", [P, N]), sb("fc", [P, N]), sb("c", [P, N])
        c_hi, c_lo = sb("c_hi", [P, N], F32R), sb("c_lo", [P, N], F32R)
        x1 = sb("x1", [P, 2, NT, P])
        z_rows = sb("z_rows", [P, 2, NT, P])
        res = sb("res", [P, 2, NT, P])
        a = sb("a", [P, N])
        a_hi, a_lo = sb("a_hi", [P, 2, N + 2], F32R), sb("a_lo", [P, 2, N + 2], F32R)
        k_sb, kv, s_sb = sb("k_sb", [P, N]), sb("kv", [P, N]), sb("s_sb", [P, N])
        r_sb, ro = sb("r_sb", [P, N]), sb("ro", [P, N])

        bank = [ctx.enter_context(nc.psum_tensor(f"bank{i}", [P, N], F32)) for i in range(8)]
        ps_t0 = bank[0:2]
        ps_t = bank[0]
        ps_h = bank[1:8] + bank[5:6]
        ps_start = bank[5]
        ps_half = [bank[2:5], bank[5:8]]
        ps_k, ps_v, ps_r, ps_o = bank[1], bank[2], bank[3], bank[4]
        ps_gate = bank[5:8]
        ps_last = bank[1:5] + bank[0:1] + bank[5:8]

        S = {}

        def s(name):
            if name not in S:
                S[name] = sem(name)
            return S[name]

        V = {n: v_cols[:, i:i + 1] for i, n in enumerate(VECTORS)}
        gate_bias = [V["bi"], V["bc"], V["bf"]]

        def bias(t, g):
            return start_bias[:, g:g + 1] if t == 0 else gate_bias[g]

        gate_fn = [ACT.Sigmoid, ACT.Tanh, ACT.Sigmoid]

        def wait(eng, name, value):
            if value <= 0:
                return
            eng.wait_ge(s(name), value)

        def half_tiles(hf):
            return slice(hf * NT // 2, (hf + 1) * NT // 2)

        def half_name(name, hf):
            return name if hf else name + "_first"

        def flat(tile):
            return tile.rearrange("p n d -> p (n d)")

        block = ctx.enter_context(nc.Block())

        def load_weights(eng, group):
            part = slice(4 * group, 4 * group + 4)
            eng.dma_start(w_t[:, part], weights[:, part]).then_inc(s(f"w{group}_loaded"), 16)

        @block.sync
        def _(sp):
            sp.dma_start(X[:, 0], x[0]).then_inc(s("x0_loaded"), 16)
            load_weights(sp, 0)
            sp.dma_start(X[:, 1], x[1]).then_inc(s("x1_loaded"), 16)
            for t in range(2, T):
                sp.dma_start(X[:, t], x[t]).then_inc(s(f"x{t}_loaded"), 16)
            load_weights(sp, 2)

            for t in range(T):
                sp.wait_ge(s("out_ready"), t + 1)
                sp.dma_start(out[t], X[:, t]).then_inc(s("stored"), 16)
            sp.wait_ge(s("stored"), 16 * T)

        @block.scalar
        def _(act):
            sc_e = nc.scalar
            act.dma_start(v_cols[:], vectors).then_inc(s("v_loaded"), 16)
            load_weights(act, 1)

            def normalise(dst, src, ln, par, scale_at, bias_at, done, tiles=range(NT), shared=False):
                for n in tiles:
                    i = sc_e.activation(dst[:, n], src[:, n], ACT.Identity,
                                        scale=sc[:, ln, par, scale_at, n:n + 1], bias=sc[:, ln, par, bias_at, n:n + 1])
                if n == NT - 1 or shared:
                    i.then_inc(s(done), 1)

            act.wait_ge(s("v_loaded"), 16)
            sc_e.activation(decay[:], V["decay_w"], ACT.Sigmoid).then_inc(s("decay_ready"), 1)
            act.wait_ge(s("w1_loaded"), 16)
            sc_e.activation(flat(wc_hi[:]), flat(w_t[:, 4:8]), ACT.Copy).then_inc(s("wc_hi"), 1)

            def y0(t, par, tiles=range(NT)):
                if t >= T:
                    return
                wait(act, "sc0", t + 1)
                wait(act, "t0", t - 1)
                normalise(y_rows[:, par], X[:, t], 0, par, 1, 3, "y0", tiles, shared=t == 1)

            def hi0(t, par):
                if t >= T:
                    return
                wait(act, "t0", t + 1)
                sc_e.activation(x_hi[:, t], ps_t0[par][:], ACT.Copy).then_inc(s("x0_hi"), 1)

            for hf in range(2):
                wait(act, half_name("sc0", hf), 1)
                for n in range(NT)[half_tiles(hf)]:
                    i = sc_e.activation(y_rows[:, 0, n], X[:, 0, n], ACT.Identity,
                                        scale=sc[:, 0, 0, 1, n:n + 1], bias=sc[:, 0, 0, 3, n:n + 1])
                i.then_inc(s(half_name("y0", hf)), 1)
                wait(act, half_name("t0", hf), 1)
                sc_e.activation(x_hi[:, 0, hf * HALF:(hf + 1) * HALF], ps_t0[hf][:, :HALF],
                                ACT.Copy).then_inc(s(half_name("x0_hi", hf)), 1)
            act.wait_ge(s("start_bias"), 1)

            def slot0(t, par):
                first = t == 0
                for hf in range(2):
                    cols = slice(hf * HALF, (hf + 1) * HALF)
                    for g in range(GATES):
                        wait(act, f"gate1_mm{hf}", GATES * t + g + 1)
                        wait(act, f"ig1_{hf}" if g < 2 else f"fc1_{hf}", t)
                        sc_e.activation(gate[:, g, cols], ps_half[hf][g][:, :HALF], gate_fn[g],
                                        bias=bias(t, g)).then_inc(s(f"gate1_{hf}"), 1)
                    if hf == 0 and first:
                        y0(1, 1, range(NT // 2))
                    elif hf == 0:
                        hi0(t + 1, 1 - par)
                        y0(t + 2, par, range(NT // 2, NT))
                    elif first:
                        hi0(1, 1)
                        y0(2, 0)
                    if hf == 1:
                        y0(t + 3, 1 - par, range(NT // 2))

            for t in range(T):
                slot0(t, t % 2)

            def tanh1(t):
                wait(act, "h1_mm", t + 1)
                sc_e.activation(H[:, t], ps_h[t][:], ACT.Tanh, bias=V["bo"]).then_inc(s("h1"), 1)

            def z1(t, par, tiles=range(NT)):
                wait(act, "sc1", t + 1)
                wait(act, "t1", t - 1)
                normalise(z_rows[:, par], x1[:, par], 1, par, 1, 3, "z1", tiles, shared=t == 0)

            def a1(t, par):
                wait(act, "t1", t + 1)
                wait(act, "a_lo", t)
                wait(act, "r_mm", t - 1)
                ps = ps_t if t < 2 else ps_r
                sc_e.activation(a[:], ps[:], ACT.Identity, scale=V["ln_w"], bias=V["ln_b"]).then_inc(s("a"), 1)
                if t == 0:
                    return
                sc_e.activation(a_hi[:, par, 2:], ps[:], ACT.Identity, scale=V["ln_w"],
                                bias=V["ln_b"]).then_inc(s("a_hi"), 1)

            for t in range(4):
                tanh1(t)
            z1(0, 0, range(NT // 2))
            tanh1(4)
            a1(0, 0)
            tanh1(5)

            def slot1(t, par):
                tp, qpar = t - 1, 1 - par
                now = t < T
                nxt = t + 1 < T
                before = t >= 1
                if nxt and before:
                    z1(t + 1, qpar, range(NT // 2))
                if now:
                    wait(act, "k_mm", t + 1)
                    wait(act, "kv", t)
                    sc_e.activation(k_sb[:], ps_k[:], ACT.Copy).then_inc(s("k"), 1)
                if nxt:
                    z1(t + 1, qpar, range(NT // 2, NT) if before else range(NT))
                if before:
                    wait(act, "sc2", tp + 1)
                    wait(act, "t2", tp - 1)
                    normalise(y_rows[:, qpar], X[:, tp], 2, qpar, 1, 3, "y2", range(NT) if now else range(NT // 2),
                              shared=not now)
                if now:
                    wait(act, "r_mm", t + 1)
                    wait(act, "ro", t)
                    sc_e.activation(r_sb[:], ps_r[:], ACT.Sigmoid).then_inc(s("r"), 1)
                if before:
                    wait(act, "t2", tp + 1)
                    sc_e.activation(x_hi[:, tp], ps_t[:], ACT.Copy).then_inc(s("x2_hi"), 1)
                if nxt:
                    a1(t + 1, qpar)
                if before:
                    for g in range(GATES):
                        wait(act, "gate2_mm", GATES * tp + g + 1)
                        wait(act, "ig2" if g < 2 else "fc2", tp)
                        sc_e.activation(gate[:, g], ps_gate[g][:], gate_fn[g],
                                        bias=bias(tp, g)).then_inc(s("gate2"), 1)
                else:
                    tanh1(6)
                    tanh1(7)

            for t in range(T + 1):
                slot1(t, t % 2)

            for t in range(T):
                wait(act, "h2_mm", t + 1)
                sc_e.activation(H[:, t], ps_last[t][:], ACT.Tanh, bias=V["bo"]).then_inc(s("h2"), 1)

        @block.gpsimd
        def _(pool):
            g_e = nc.gpsimd
            g_e.memset(ident[:], 0.0).then_inc(s("pool_init"), 1)
            g_e.memset(minus_half[:], -0.5).then_inc(s("pool_init"), 1)
            pool.wait_ge(s("pool_init"), 2)
            g_e.affine_select(out=ident[:], in_=ident[:], compare_op=ALU.not_equal, fill=1.0,
                              base=0, pattern=[[-1, P]], channel_multiplier=1).then_inc(s("ident_ready"), 1)

            def scalars(ln, t, par, own, done, used, tiles=slice(0, NT)):
                mean, var = mv[:, ln, par, tiles, 0], mv[:, ln, par, tiles, 1]
                q = [sc[:, ln, par, i, tiles] for i in range(8)]
                wait(pool, used, t - 1)
                before = (6 if ln == 1 else 3) * t
                by, plus = (1.0 + EPS, EPS * EPS) if ln == 1 else (1.0, EPS)
                g_e.tensor_scalar(q[0], var, by, plus, ALU.mult, ALU.add).then_inc(s(own), 1)
                g_e.tensor_scalar(q[2], mean, -1.0, 0.0, ALU.mult, ALU.add).then_inc(s(own), 1)
                wait(pool, own, before + 2)
                g_e.tensor_tensor(q[1], q[0], minus_half[:, tiles], ALU.pow).then_inc(s(own), 1)
                wait(pool, own, before + 3)
                g_e.tensor_tensor(q[3], q[2], q[1], ALU.mult).then_inc(s(done), 1)
                if ln == 1:
                    g_e.tensor_scalar(q[4], var, 1.0, EPS, ALU.mult, ALU.add).then_inc(s(own), 1)
                    wait(pool, own, before + 4)
                    g_e.tensor_tensor(q[7], q[4], minus_half[:], ALU.pow).then_inc(s(own), 1)
                    wait(pool, own, before + 5)
                    g_e.tensor_tensor(q[6], q[2], q[7], ALU.mult).then_inc(s(own), 1)
                    g_e.tensor_scalar(q[5], q[7], 1.0, 1.0, ALU.mult, ALU.add).then_inc(s("sc1b"), 1)
                    wait(pool, own, before + 6)

            def sc0(t, par):
                if t >= T:
                    return
                wait(pool, "mv0", t + 1)
                scalars(0, t, par, "own0", "sc0", "y0")

            for hf in range(2):
                wait(pool, half_name("mv0", hf), 1)
                scalars(0, 0, 0, half_name("own0", hf), half_name("sc0", hf), "y0", half_tiles(hf))
            sc0(1, 1)

            def mix_part(t):
                if t == 1:
                    pool.wait_ge(s("w2_loaded"), 16)
                    pool.wait_ge(s("tm_ready"), 1)
                if t in (1, 2, 3):
                    j = t - 1
                    for prev in range(2):
                        i = g_e.tensor_scalar(mix[:, 2 * j + prev], w_t[:, 8 + j],
                                              tm_cols[:, 2 * j + prev:2 * j + prev + 1], 0.0, ALU.mult, ALU.add)
                    if j == 2:
                        i.then_inc(s("mix_ready"), 1)
                if t == 5:
                    g_e.tensor_scalar(flat(mix_hi[:]), flat(mix[:]), 1.0, 0.0, ALU.mult,
                                      ALU.add).then_inc(s("mix_hi"), 1)
                if t == 6:
                    pool.wait_ge(s("mix_hi"), 1)
                    g_e.tensor_tensor(flat(mix_lo[:]), flat(mix[:]), flat(mix_hi[:]).bitcast(F32),
                                      ALU.subtract).then_inc(s("mix_lo"), 1)

            def slot0(t, par):
                if t == 5:
                    pool.wait_ge(s("mix_ready"), 1)
                for hf in range(2):
                    cols = slice(hf * HALF, (hf + 1) * HALF)
                    wait(pool, f"gate1_{hf}", GATES * t + 2)
                    wait(pool, f"c1_{hf}", t)
                    g_e.tensor_tensor(ig[:, cols], gate[:, 0, cols], gate[:, 1, cols],
                                      ALU.mult).then_inc(s(f"ig1_{hf}"), 1)
                    if hf == 0:
                        if t == 0:
                            sc0(2, 0)
                        sc0(t + 3, 1 - t % 2)
                mix_part(t)

            for t in range(T):
                slot0(t, t % 2)

            def res1(t, par):
                wait(pool, "sc1b", t + 1)
                wait(pool, "x2", t - 1)
                for n in range(NT):
                    i = g_e.tensor_scalar(res[:, par, n], x1[:, par, n], sc[:, 1, par, 5, n:n + 1],
                                          sc[:, 1, par, 6, n:n + 1], ALU.mult, ALU.add)
                i.then_inc(s("res1"), 1)

            def sc1(t, par):
                wait(pool, "mv1", t + 1)
                scalars(1, t, par, "own1", "sc1", "z1")

            sc1(0, 0)
            res1(0, 0)
            sc1(1, 1)

            def slot1(t, par):
                tp, qpar = t - 1, 1 - par
                nxt = t + 1 < T
                nxt2 = t + 2 < T
                before = t >= 1
                if before:
                    wait(pool, "mv2", tp + 1)
                    scalars(2, tp, qpar, "own2", "sc2", "y2")
                if t == T:
                    wait(pool, "sc2", T)
                    wait(pool, "t2", tp - 1)
                    for n in range(NT // 2, NT):
                        i = g_e.tensor_scalar(y_rows[:, qpar, n], X[:, tp, n], sc[:, 2, qpar, 1, n:n + 1],
                                              sc[:, 2, qpar, 3, n:n + 1], ALU.mult, ALU.add)
                    i.then_inc(s("y2_rest"), 1)
                if nxt:
                    res1(t + 1, qpar)
                if nxt2:
                    sc1(t + 2, par)
                if before and tp < T - 2:
                    wait(pool, "gate2", GATES * tp + 2)
                    wait(pool, "c2", tp)
                    g_e.tensor_tensor(ig[:], gate[:, 0], gate[:, 1], ALU.mult).then_inc(s("ig2"), 1)

            for t in range(T + 1):
                slot1(t, t % 2)

        @block.vector
        def _(dve):
            v_e = nc.vector

            def stats(src, ln, t, par, own, done, used):
                wait(dve, used, t - 1)
                for n in range(NT):
                    i = v_e.bn_stats(bn[:, ln, par, n], src[:, n])
                i.then_inc(s(own), 1)
                wait(dve, own, t + 1)
                for n in range(NT):
                    i = v_e.bn_aggr(mv[:, ln, par, n], bn[:, ln, par, n])
                i.then_inc(s(done), 1)

            def bn_part(src, ln, par, n, own):
                i = v_e.bn_stats(bn[:, ln, par, n], src[:, n])
                if n == NT - 1:
                    i.then_inc(s(own), 1)

            def aggregate_part(ln, par, n, done):
                i = v_e.bn_aggr(mv[:, ln, par, n], bn[:, ln, par, n])
                if n == NT - 1:
                    i.then_inc(s(done), 1)

            def stats0(t, par):
                if t >= T:
                    return
                wait(dve, f"x{t}_loaded", 16)
                stats(X[:, t], 0, t, par, "bn0", "mv0", "sc0")

            def normalise_rest(dst, src, ln, par):
                for n in range(NT // 2, NT):
                    i = v_e.tensor_scalar(dst[:, n], src[:, n], sc[:, ln, par, 1, n:n + 1], sc[:, ln, par, 3, n:n + 1],
                                          ALU.mult, ALU.add)
                return i

            def lo0(t, par):
                if t >= T:
                    return
                wait(dve, "x0_hi", t + 1)
                v_e.tensor_tensor(x_lo[:, t], ps_t0[par][:], x_hi[:, t].bitcast(F32),
                                  ALU.subtract).then_inc(s("x0_lo"), 1)

            v_e.memset(zeros[:], 0.0)
            v_e.memset(a_hi[:, :, 0:2].bitcast(F32), 0.0)
            v_e.memset(a_lo[:, :, 0:2].bitcast(F32), 0.0).then_inc(s("pad_ready"), 1)
            wait(dve, "x0_loaded", 16)
            for hf in range(2):
                for n in range(NT)[half_tiles(hf)]:
                    i = v_e.bn_stats(bn[:, 0, 0, n], X[:, 0, n])
                i.then_inc(s(half_name("bn0", hf)), 1)
                wait(dve, half_name("bn0", hf), 1)
                for n in range(NT)[half_tiles(hf)]:
                    i = v_e.bn_aggr(mv[:, 0, 0, n], bn[:, 0, 0, n])
                i.then_inc(s(half_name("mv0", hf)), 1)
            dve.wait_ge(s("w0_loaded"), 16)
            v_e.tensor_copy(flat(wx_hi[:]), flat(w_t[:, 0:4])).then_inc(s("wx_hi"), 1)
            dve.wait_ge(s("wx_hi"), 1)
            v_e.tensor_tensor(flat(wx_lo[:]), flat(w_t[:, 0:4]), flat(wx_hi[:]).bitcast(F32),
                              ALU.subtract).then_inc(s("wx_ready"), 1)
            stats0(1, 1)
            dve.wait_ge(s("wc_hi"), 1)
            v_e.tensor_tensor(flat(wc_lo[:]), flat(w_t[:, 4:8]), flat(wc_hi[:]).bitcast(F32),
                              ALU.subtract).then_inc(s("wc_ready"), 1)

            def lo0_half(hf):
                cols = slice(hf * HALF, (hf + 1) * HALF)
                wait(dve, half_name("x0_hi", hf), 1)
                v_e.tensor_tensor(x_lo[:, 0, cols], ps_t0[hf][:, :HALF], x_hi[:, 0, cols].bitcast(F32),
                                  ALU.subtract).then_inc(s(half_name("x0_lo", hf)), 1)

            lo0_half(0)
            dve.wait_ge(s("v_loaded"), 16)
            dve.wait_ge(s("start_mm"), 1)
            v_e.tensor_tensor(start_bias[:], ps_start[:, 0:GATES], v_cols[:, 0:GATES],
                              ALU.add).then_inc(s("start_bias"), 1)
            stats0(2, 0)
            lo0_half(1)
            wait(dve, "sc0", 2)
            normalise_rest(y_rows[:, 1], X[:, 1], 0, 1).then_inc(s("y0_rest"), 1)
            stats0(3, 1)

            def mixing_factors():
                for j, name in enumerate(("tmk", "tmv", "tmr")):
                    v_e.tensor_copy(tm_cols[:, 2 * j:2 * j + 1], V[name])
                    i = v_e.tensor_scalar(tm_cols[:, 2 * j + 1:2 * j + 2], V[name], -1.0, 1.0, ALU.mult, ALU.add)
                i.then_inc(s("tm_ready"), 1)

            def forget(t, cols):
                if t == 0:
                    return v_e.tensor_scalar(fc[:, cols], gate[:, 2, cols], V["in_c"], 0.0, ALU.mult, ALU.add)
                return v_e.tensor_tensor(fc[:, cols], gate[:, 2, cols], c[:, cols], ALU.mult)

            def slot0(t, par):
                ahead = t > 0 and t + 4 < T
                for hf in range(2):
                    cols = slice(hf * HALF, (hf + 1) * HALF)

                    def between(n):
                        if ahead and hf == 0:
                            bn_part(X[:, t + 4], 0, par, n, "bn0")
                        elif ahead and n < 2:
                            wait(dve, "sc0", t + 3)
                            aggregate_part(0, par, 2 * n, "mv0")
                            aggregate_part(0, par, 2 * n + 1, "mv0")
                    if ahead:
                        if hf == 0:
                            wait(dve, f"x{t + 4}_loaded", 16)
                        else:
                            wait(dve, "bn0", t + 5)
                    wait(dve, f"gate1_{hf}", GATES * (t + 1))
                    forget(t, cols).then_inc(s(f"fc1_{hf}"), 1)
                    between(0)
                    wait(dve, f"fc1_{hf}", t + 1)
                    wait(dve, f"ig1_{hf}", t + 1)
                    v_e.tensor_tensor(c[:, cols], fc[:, cols], ig[:, cols], ALU.add).then_inc(s(f"c1_{hf}"), 1)
                    if hf == 0 and t > 0:
                        lo0(t + 1, 1 - par)
                    between(1)
                    wait(dve, f"c1_{hf}", t + 1)
                    v_e.tensor_copy(c_hi[:, cols], c[:, cols]).then_inc(s(f"c1_hi{hf}"), 1)
                    between(2)
                    wait(dve, f"c1_hi{hf}", t + 1)
                    v_e.tensor_tensor(c_lo[:, cols], c[:, cols], c_hi[:, cols].bitcast(F32),
                                      ALU.subtract).then_inc(s(f"c1_lo{hf}"), 1)
                    between(3)
                    if hf == 0 and t == 0:
                        lo0(1, 1)
                        stats0(4, 0)
                if t == 0:
                    mixing_factors()

            for t in range(T):
                slot0(t, t % 2)

            def front1(t, par):
                wait(dve, "th", t + 1)
                wait(dve, "res1", t - 1)
                wait(dve, "z1", t - 1)
                v_e.scalar_tensor_tensor(out=flat(x1[:, par]), in0=ps_t[:], scalar=0.5, in1=flat(X[:, t]),
                                         op0=ALU.mult, op1=ALU.add).then_inc(s("x1"), 1)

            def stats1(t, par):
                wait(dve, "x1", t + 1)
                stats(x1[:, par], 1, t, par, "bn1", "mv1", "sc1b")

            def low_a(t, par):
                wait(dve, "a_hi", t + 1)
                wait(dve, "r_mm", t - 1)
                v_e.tensor_tensor(a_lo[:, par, 2:], a[:], a_hi[:, par, 2:].bitcast(F32),
                                  ALU.subtract).then_inc(s("a_lo"), 1)

            front1(0, 0)
            stats1(0, 0)
            front1(1, 1)
            stats1(1, 1)
            dve.wait_ge(s("sc1"), 1)
            normalise_rest(z_rows[:, 0], x1[:, 0], 1, 0).then_inc(s("z1_rest"), 1)
            dve.wait_ge(s("a"), 1)
            v_e.tensor_copy(a_hi[:, 0, 2:], a[:]).then_inc(s("a_hi"), 1)
            low_a(0, 0)

            def c_new(t):
                wait(dve, "fc2", t + 1)
                wait(dve, "ig2", t + 1)
                v_e.tensor_tensor(c[:], fc[:], ig[:], ALU.add).then_inc(s("c2"), 1)

            def c_high(t):
                wait(dve, "c2", t + 1)
                if t == 0:
                    wait(dve, "h1_mm", T)
                v_e.tensor_copy(c_hi[:], c[:]).then_inc(s("c2_hi"), 1)

            def c_rest(t):
                wait(dve, "c2_hi", t + 1)
                v_e.tensor_tensor(c_lo[:], c[:], c_hi[:].bitcast(F32), ALU.subtract).then_inc(s("c2_lo"), 1)

            def slot1(t, par):
                tp, qpar = t - 1, 1 - par
                now = t < T
                nxt = t + 1 < T
                nxt2 = t + 2 < T
                before = t >= 1
                before2 = t >= 2
                if before2:
                    c_new(t - 2)
                    c_high(t - 2)
                    if not now:
                        c_rest(t - 2)
                if t == 0:
                    front1(2, 0)
                    stats1(2, 0)
                if t == 1:
                    front1(3, 1)
                if now:
                    wait(dve, "k", t + 1)
                    wait(dve, "v_mm", t + 1)
                    v_e.tensor_tensor(kv[:], ps_v[:], k_sb[:], ALU.mult).then_inc(s("kv"), 1)
                    wait(dve, "kv", t + 1)
                    wait(dve, "o_mm", t)
                    v_e.tensor_tensor_scan(s_sb[:], decay[:, 0:1].to_broadcast([P, N]), kv[:], 0.0,
                                           ALU.mult, ALU.add).then_inc(s("scan"), 1)
                if nxt2 and before2:
                    front1(t + 2, par)
                if now and before2:
                    c_rest(t - 2)
                if nxt2 and before:
                    stats1(t + 2, par)
                if now:
                    wait(dve, "o_mm", t + 1)
                    wait(dve, "r", t + 1)
                    wait(dve, "t3", t)
                    v_e.tensor_tensor(ro[:], ps_o[:], r_sb[:], ALU.mult).then_inc(s("ro"), 1)
                if before:
                    wait(dve, "x2_hi", tp + 1)
                    v_e.tensor_tensor(x_lo[:, tp], ps_t[:], x_hi[:, tp].bitcast(F32),
                                      ALU.subtract).then_inc(s("x2_lo"), 1)
                if nxt:
                    low_a(t + 1, qpar)
                if now:
                    wait(dve, "t3", t + 1)
                    wait(dve, "res1", t + 1)
                    v_e.tensor_tensor(flat(X[:, t]), ps_o[:], flat(res[:, par]), ALU.add).then_inc(s("x2"), 1)
                    wait(dve, "sc2", t - 1)
                    wait(dve, "x2", t + 1)
                    for n in range(NT):
                        bn_part(X[:, t], 2, par, n, "bn2")
                    wait(dve, "bn2", t + 1)
                    for n in range(NT):
                        aggregate_part(2, par, n, "mv2")
                if before:
                    if tp >= T - 2:
                        wait(dve, "gate2", GATES * tp + 2)
                        v_e.tensor_tensor(ig[:], gate[:, 0], gate[:, 1], ALU.mult).then_inc(s("ig2"), 1)
                    wait(dve, "gate2", GATES * (tp + 1))
                    forget(tp, slice(0, N)).then_inc(s("fc2"), 1)

            for t in range(T + 1):
                slot1(t, t % 2)
            c_new(T - 1)
            c_high(T - 1)
            c_rest(T - 1)

            for t in range(T):
                wait(dve, "th2", t + 1)
                v_e.scalar_tensor_tensor(out=flat(X[:, t]), in0=ps_last[t][:], scalar=0.5, in1=flat(X[:, t]),
                                         op0=ALU.mult, op1=ALU.add).then_inc(s("out_ready"), 1)

        @block.tensor
        def _(pe):
            t_e = nc.tensor

            def product3(dst, w_hi, w_lo, r_hi, r_lo, start, stop):
                t_e.matmul(dst, w_hi, r_hi, start=start, stop=False)
                t_e.matmul(dst, w_lo, r_hi, start=False, stop=False)
                return t_e.matmul(dst, w_hi, r_lo, start=False, stop=stop)

            def transpose4(dst, src):
                for n in range(NT):
                    i = t_e.transpose(dst[:, n * P:(n + 1) * P], src[:, n], ident[:])
                return i

            pe.wait_ge(s("ident_ready"), 1)

            def t0(t, par):
                if t >= T:
                    return
                wait(pe, "y0", t + 1)
                if t == 1:
                    wait(pe, "y0_rest", 1)
                wait(pe, "x0_lo", t - 1 if t > 1 else 1)
                transpose4(ps_t0[par], y_rows[:, par]).then_inc(s("t0"), 1)

            pe.wait_ge(s("pad_ready"), 1)
            def warm_up(bank, times):
                for n in range(times):
                    t_e.matmul(bank[:], ident[:], flat(zeros[:]), start=True, stop=True)

            warm_up(ps_half[1][2], WARM)
            def t0_half(hf):
                wait(pe, half_name("y0", hf), 1)
                for n in range(NT // 2):
                    i = t_e.transpose(ps_t0[hf][:, n * P:(n + 1) * P], y_rows[:, 0, hf * NT // 2 + n], ident[:])
                i.then_inc(s(half_name("t0", hf)), 1)

            t0_half(0)
            pe.wait_ge(s("w1_loaded"), 16)
            pe.wait_ge(s("v_loaded"), 16)
            for g in range(GATES):
                i = t_e.matmul(ps_start[:, g:g + 1], w_t[:, 4 + g], V["in_c"], start=True, stop=True)
            i.then_inc(s("start_mm"), 1)
            t0_half(1)
            pe.wait_ge(s("wx_ready"), 1)

            def slot0(t, par):
                first = t == 0
                for hf in range(2):
                    if first:
                        wait(pe, half_name("x0_lo", hf), 1)
                        if hf == 1:
                            wait(pe, "start_bias", 1)
                    elif hf == 0:
                        wait(pe, "x0_lo", t + 1)
                    cols = slice(hf * HALF, (hf + 1) * HALF)
                    for g in range(GATES):
                        wait(pe, f"gate1_{hf}", GATES * (t - 1) + g + 1 if t else 0)
                        i = product3(ps_half[hf][g][:, :HALF], wx_hi[:, g], wx_lo[:, g],
                                     x_hi[:, t, cols], x_lo[:, t, cols], True, first)
                        if first:
                            i.then_inc(s(f"gate1_mm{hf}"), 1)
                    wait(pe, f"c1_lo{hf}", t)
                    for g in range(0 if first else GATES):
                        product3(ps_half[hf][g][:, :HALF], wc_hi[:, g], wc_lo[:, g], c_hi[:, cols], c_lo[:, cols],
                                 False, True).then_inc(s(f"gate1_mm{hf}"), 1)
                    if (t, hf) in ((0, 1), (1, 0)):
                        t0(t + 1, 1 - par)
                if not first:
                    t0(t + 2, par)
                if first:
                    warm_up(ps_t0[0], 2)
                    pe.wait_ge(s("wc_ready"), 1)

            for t in range(T):
                slot0(t, t % 2)

            def out1_x(t):
                if t == T - 1:
                    wait(pe, "h1", t - 2)
                product3(ps_h[t][:], wx_hi[:, 3], wx_lo[:, 3], x_hi[:, t], x_lo[:, t], True, False)

            def out1_c(t):
                product3(ps_h[t][:], wc_hi[:, 3], wc_lo[:, 3], c_hi[:], c_lo[:], False,
                         True).then_inc(s("h1_mm"), 1)

            def th(t):
                wait(pe, "h1", t + 1)
                if t < 4:
                    wait(pe, "x1", t)
                    if t >= 2:
                        wait(pe, "a_hi", t - 1)
                else:
                    wait(pe, "x2_lo", t - 3)
                transpose4(ps_t, H[:, t].rearrange("p (n d) -> p n d", n=NT)).then_inc(s("th"), 1)

            pe.wait_ge(s("gate1_0"), GATES * T)
            for t in range(3):
                out1_x(t)
            pe.wait_ge(s("c1_lo0"), T)
            pe.wait_ge(s("c1_lo1"), T)
            out1_c(0)
            out1_c(1)
            th(0)
            out1_c(2)
            th(1)
            pe.wait_ge(s("gate1_1"), GATES * T)
            for t in range(3, 5):
                out1_x(t)
                out1_c(t)
            out1_x(5)

            def t1(t, par):
                wait(pe, "z1", t + 1)
                if t == 0:
                    wait(pe, "z1_rest", 1)
                if t < 2:
                    wait(pe, "x1", t + 2)
                else:
                    wait(pe, "r", t)
                ps = ps_t if t < 2 else ps_r
                transpose4(ps, z_rows[:, par]).then_inc(s("t1"), 1)

            def mixed(dst, j, par, done):
                row, prev = slice(2, N + 2), slice(1, N + 1)
                product3(dst, mix_hi[:, 2 * j], mix_lo[:, 2 * j], a_hi[:, par, row], a_lo[:, par, row], True, False)
                product3(dst, mix_hi[:, 2 * j + 1], mix_lo[:, 2 * j + 1], a_hi[:, par, prev], a_lo[:, par, prev],
                         False, True).then_inc(s(done), 1)

            t1(0, 0)
            out1_c(5)
            th(2)
            out1_x(6)
            pe.wait_ge(s("pad_ready"), 1)
            pe.wait_ge(s("mix_lo"), 1)
            pe.wait_ge(s("h1"), 4)

            def attention_rows(t):
                wait(pe, "ro", t + 1)
                transpose4(ps_o, ro.rearrange("p (n d) -> p n d", n=NT)).then_inc(s("t3"), 1)

            def slot1(t, par):
                tp, qpar = t - 1, 1 - par
                now = t < T
                nxt = t + 1 < T
                nxt2 = t + 2 < T
                before = t >= 1
                if t == 1:
                    th(3)
                if now:
                    wait(pe, "a_lo", t + 1)
                    wait(pe, "k", t)
                    mixed(ps_k[:], 0, par, "k_mm")
                    wait(pe, "kv", t)
                    mixed(ps_v[:], 1, par, "v_mm")
                    mixed(ps_r[:], 2, par, "r_mm")
                    if t == 0:
                        t1(1, 1)
                        out1_c(6)
                    elif nxt2 and t > 1:
                        th(t + 2)
                    wait(pe, "scan", t + 1)
                    wait(pe, "x2", t)
                    t_e.matmul(ps_o[:], w_t[:, 11], s_sb[:], start=True, stop=True).then_inc(s("o_mm"), 1)
                if before:
                    if not now:
                        for n in range(3):
                            out2_x(n)
                    wait(pe, "y2", tp + 1)
                    if not now:
                        wait(pe, "y2_rest", 1)
                    if nxt2:
                        wait(pe, "x1", t + 3)
                    else:
                        wait(pe, "x2_lo", tp)
                    transpose4(ps_t, y_rows[:, qpar]).then_inc(s("t2"), 1)
                    if not now:
                        out2_x(3)
                if nxt and before:
                    t1(t + 1, qpar)
                if before:
                    wait(pe, "c2_lo", tp)
                    for g in range(0 if tp == 0 else GATES):
                        if t == T - 1 and g == 1:
                            attention_rows(t)
                        wait(pe, "gate2", GATES * (tp - 1) + g + 1)
                        product3(ps_gate[g][:], wc_hi[:, g], wc_lo[:, g], c_hi[:], c_lo[:], True, False)
                if t == 0:
                    out1_x(7)
                if now and t < T - 1:
                    attention_rows(t)
                if t == 0:
                    out1_c(7)
                if before:
                    wait(pe, "x2_lo", tp + 1)
                    for g in range(GATES):
                        product3(ps_gate[g][:], wx_hi[:, g], wx_lo[:, g], x_hi[:, tp], x_lo[:, tp],
                                 tp == 0, True).then_inc(s("gate2_mm"), 1)

            def out2_x(t):
                product3(ps_last[t][:], wx_hi[:, 3], wx_lo[:, 3], x_hi[:, t], x_lo[:, t], True, False)

            for t in range(T + 1):
                slot1(t, t % 2)

            out2_x(4)
            for g in range(GATES):
                wait(pe, "gate2", GATES * (T - 1) + g + 1)
                out2_x(5 + g)

            def out2_c(t, parts):
                if 0 in parts:
                    t_e.matmul(ps_last[t][:], wc_hi[:, 3], c_hi[:], start=False, stop=False)
                    t_e.matmul(ps_last[t][:], wc_lo[:, 3], c_hi[:], start=False, stop=False)
                if 1 in parts:
                    t_e.matmul(ps_last[t][:], wc_hi[:, 3], c_lo[:], start=False,
                               stop=True).then_inc(s("h2_mm"), 1)

            pe.wait_ge(s("c2_hi"), T)
            out2_c(0, [0])
            out2_c(1, [0])
            pe.wait_ge(s("c2_lo"), T)
            out2_c(0, [1])
            out2_c(1, [1])
            for t in range(T):
                if t + 2 < T:
                    out2_c(t + 2, [0, 1])
                wait(pe, "h2", t + 1)
                transpose4(ps_last[t], H[:, t].rearrange("p (n d) -> p n d", n=NT)).then_inc(s("th2"), 1)


_WEIGHTS = {"wi": "L0_ffn_wi", "wc": "L0_ffn_wc", "wf": "L0_ffn_wf", "wo": "L0_ffn_wo",
            "ui": "L0_ffn_ui", "uc": "L0_ffn_uc", "uf": "L0_ffn_uf", "uo": "L0_ffn_uo",
            "Wk": "L0_attn_Wk", "Wv": "L0_attn_Wv", "Wr": "L0_attn_Wr", "Wo": "L0_attn_Wo"}
_VECTORS = {"bi": "L0_ffn_bi", "bc": "L0_ffn_bc", "bf": "L0_ffn_bf", "bo": "L0_ffn_bo", "in_c": "L0_ffn_in_c",
            "decay_w": "L0_attn_decay_w", "ln_w": "L0_attn_ln_w", "ln_b": "L0_attn_ln_b",
            "tmk": "L0_attn_tmk", "tmv": "L0_attn_tmv", "tmr": "L0_attn_tmr"}


def kernel(**inputs):
    import numpy as np
    import concourse.bacc as bacc
    from concourse.bass_utils import run_bass_kernel_spmd

    nc = bacc.Bacc("TRN2", target_bir_lowering=False, num_devices=1)
    arrays = {}

    def dram(name, array):
        arrays[name] = np.ascontiguousarray(array)
        return nc.dram_tensor(name, arrays[name].shape, mybir.dt.from_np(arrays[name].dtype), kind="ExternalInput").ap()

    x = dram("x", inputs["L0_attn_x"].reshape(T, NT, P, P).transpose(0, 2, 1, 3))
    weights = dram("weights", np.stack([inputs[_WEIGHTS[k]] for k in WEIGHTS]).transpose(2, 0, 1))
    vectors = dram("vectors", np.stack([inputs[_VECTORS[k]] for k in VECTORS], axis=1))
    out = nc.dram_tensor("out", (T, P, NT, P), F32, kind="ExternalOutput").ap()
    macaron_kernel(nc, x, out, weights, vectors)
    r = run_bass_kernel_spmd(nc, [arrays], core_ids=[0])
    return np.ascontiguousarray(r.results[0]["out"].transpose(0, 2, 1, 3)).reshape(T, N, P)
```
